# Optimizing a Trainium2 kernel written in Bass

```python
import numpy as np
import jax
import jax.numpy as jnp

def _softmax(x, axis=-1):
    return jax.nn.softmax(x, axis=axis)

def _gelu(x):
    return jax.nn.gelu(x, approximate=True)

def _silu(x):
    return jax.nn.silu(x)

def _sigmoid(x):
    return jax.nn.sigmoid(x)

def _layernorm(x, axis=-1, eps=1e-05):
    m = jnp.mean(x, axis=axis, keepdims=True)
    v = jnp.var(x, axis=axis, keepdims=True)
    return (x - m) / jnp.sqrt(v + eps)

def _scatter_add(tgt, idx, src, axis=0):
    return tgt.at[idx].add(src)

def _segment_sum(src, seg, n):
    return jax.ops.segment_sum(src, seg, n)
kernel_name = 'mk_dlrm_tower_d1_rec_r8_f4e223'

def setup_inputs(seed: int=0):
    np.random.seed(seed)
    _w = jnp.asarray

    def _rec_inputs():
        import jax
        import jax.numpy as jnp
        _tk = jax.random.key(seed)
        ids = jnp.stack([jax.random.randint(jax.random.fold_in(_tk, 200 + f), (512,), 0, v, jnp.int32) for f, v in enumerate([1000, 1250, 1000, 125000, 1000, 12500, 1000, 1000, 1000, 1000, 1250, 1000, 1000, 1250, 1000, 12500, 12500, 1250, 12500, 1000, 1250, 1250, 1250, 1250, 1000, 12500])], axis=1)
        tbl_0 = 0.05 * jax.random.normal(jax.random.fold_in(_tk, 500 + 0), (1000, 128), jnp.float32)
        tbl_1 = 0.05 * jax.random.normal(jax.random.fold_in(_tk, 500 + 1), (1250, 128), jnp.float32)
        tbl_2 = 0.05 * jax.random.normal(jax.random.fold_in(_tk, 500 + 2), (1000, 128), jnp.float32)
        tbl_3 = 0.05 * jax.random.normal(jax.random.fold_in(_tk, 500 + 3), (125000, 128), jnp.float32)
        tbl_4 = 0.05 * jax.random.normal(jax.random.fold_in(_tk, 500 + 4), (1000, 128), jnp.float32)
        tbl_5 = 0.05 * jax.random.normal(jax.random.fold_in(_tk, 500 + 5), (12500, 128), jnp.float32)
        tbl_6 = 0.05 * jax.random.normal(jax.random.fold_in(_tk, 500 + 6), (1000, 128), jnp.float32)
        tbl_7 = 0.05 * jax.random.normal(jax.random.fold_in(_tk, 500 + 7), (1000, 128), jnp.float32)
        tbl_8 = 0.05 * jax.random.normal(jax.random.fold_in(_tk, 500 + 8), (1000, 128), jnp.float32)
        tbl_9 = 0.05 * jax.random.normal(jax.random.fold_in(_tk, 500 + 9), (1000, 128), jnp.float32)
        tbl_10 = 0.05 * jax.random.normal(jax.random.fold_in(_tk, 500 + 10), (1250, 128), jnp.float32)
        tbl_11 = 0.05 * jax.random.normal(jax.random.fold_in(_tk, 500 + 11), (1000, 128), jnp.float32)
        tbl_12 = 0.05 * jax.random.normal(jax.random.fold_in(_tk, 500 + 12), (1000, 128), jnp.float32)
        tbl_13 = 0.05 * jax.random.normal(jax.random.fold_in(_tk, 500 + 13), (1250, 128), jnp.float32)
        tbl_14 = 0.05 * jax.random.normal(jax.random.fold_in(_tk, 500 + 14), (1000, 128), jnp.float32)
        tbl_15 = 0.05 * jax.random.normal(jax.random.fold_in(_tk, 500 + 15), (12500, 128), jnp.float32)
        tbl_16 = 0.05 * jax.random.normal(jax.random.fold_in(_tk, 500 + 16), (12500, 128), jnp.float32)
        tbl_17 = 0.05 * jax.random.normal(jax.random.fold_in(_tk, 500 + 17), (1250, 128), jnp.float32)
        tbl_18 = 0.05 * jax.random.normal(jax.random.fold_in(_tk, 500 + 18), (12500, 128), jnp.float32)
        tbl_19 = 0.05 * jax.random.normal(jax.random.fold_in(_tk, 500 + 19), (1000, 128), jnp.float32)
        tbl_20 = 0.05 * jax.random.normal(jax.random.fold_in(_tk, 500 + 20), (1250, 128), jnp.float32)
        tbl_21 = 0.05 * jax.random.normal(jax.random.fold_in(_tk, 500 + 21), (1250, 128), jnp.float32)
        tbl_22 = 0.05 * jax.random.normal(jax.random.fold_in(_tk, 500 + 22), (1250, 128), jnp.float32)
        tbl_23 = 0.05 * jax.random.normal(jax.random.fold_in(_tk, 500 + 23), (1250, 128), jnp.float32)
        tbl_24 = 0.05 * jax.random.normal(jax.random.fold_in(_tk, 500 + 24), (1000, 128), jnp.float32)
        tbl_25 = 0.05 * jax.random.normal(jax.random.fold_in(_tk, 500 + 25), (12500, 128), jnp.float32)
        _rk = jax.random.fold_in(_tk, 7)
        r_dense_features = -0.000520686 + 1.00062 * jax.random.normal(jax.random.fold_in(_rk, 101), (512, 128), jnp.float32)
        W_top1 = 0.0405887 * jax.random.normal(jax.random.fold_in(_tk, 801), (607, 512), jnp.float32)
        W_top2 = 0.0441942 * jax.random.normal(jax.random.fold_in(_tk, 802), (512, 256), jnp.float32)
        W_top3 = 0.0625 * jax.random.normal(jax.random.fold_in(_tk, 803), (256, 1), jnp.float32)
        b_top1 = jnp.zeros((512,), jnp.float32)
        b_top2 = jnp.zeros((256,), jnp.float32)
        return (r_dense_features, ids, tbl_0, tbl_1, tbl_2, tbl_3, tbl_4, tbl_5, tbl_6, tbl_7, tbl_8, tbl_9, tbl_10, tbl_11, tbl_12, tbl_13, tbl_14, tbl_15, tbl_16, tbl_17, tbl_18, tbl_19, tbl_20, tbl_21, tbl_22, tbl_23, tbl_24, tbl_25, W_top1, b_top1, W_top2, b_top2, W_top3)
    r_dense_features, ids, tbl_0, tbl_1, tbl_2, tbl_3, tbl_4, tbl_5, tbl_6, tbl_7, tbl_8, tbl_9, tbl_10, tbl_11, tbl_12, tbl_13, tbl_14, tbl_15, tbl_16, tbl_17, tbl_18, tbl_19, tbl_20, tbl_21, tbl_22, tbl_23, tbl_24, tbl_25, W_top1, b_top1, W_top2, b_top2, W_top3 = _rec_inputs()

    def _L0_rec_setup():
        import jax, jax.numpy as jnp
        import numpy as np
        F = 26
        N = F + 1
        _TRIU_I, _TRIU_J = np.triu_indices(N, k=1)
        key = jax.random.key(seed)
        k1, k2 = jax.random.split(key)
        B, D = (2048, 128)
        dense_features = jax.random.normal(k1, (B, D), dtype=jnp.float32)
        sparse_features = jax.random.normal(k2, (B, F, D), dtype=jnp.float32)
        return {'dense_features': dense_features, 'sparse_features': sparse_features}
    _L0_rec_all = _L0_rec_setup()
    _L0_rec_in = {k: v for k, v in _L0_rec_all.items() if k in ()}
    del _L0_rec_all
    return {'r_dense_features': r_dense_features, 'ids': ids, 'tbl_0': tbl_0, 'tbl_1': tbl_1, 'tbl_2': tbl_2, 'tbl_3': tbl_3, 'tbl_4': tbl_4, 'tbl_5': tbl_5, 'tbl_6': tbl_6, 'tbl_7': tbl_7, 'tbl_8': tbl_8, 'tbl_9': tbl_9, 'tbl_10': tbl_10, 'tbl_11': tbl_11, 'tbl_12': tbl_12, 'tbl_13': tbl_13, 'tbl_14': tbl_14, 'tbl_15': tbl_15, 'tbl_16': tbl_16, 'tbl_17': tbl_17, 'tbl_18': tbl_18, 'tbl_19': tbl_19, 'tbl_20': tbl_20, 'tbl_21': tbl_21, 'tbl_22': tbl_22, 'tbl_23': tbl_23, 'tbl_24': tbl_24, 'tbl_25': tbl_25, 'W_top1': W_top1, 'b_top1': b_top1, 'W_top2': W_top2, 'b_top2': b_top2, 'W_top3': W_top3}

def reference(r_dense_features, ids, tbl_0, tbl_1, tbl_2, tbl_3, tbl_4, tbl_5, tbl_6, tbl_7, tbl_8, tbl_9, tbl_10, tbl_11, tbl_12, tbl_13, tbl_14, tbl_15, tbl_16, tbl_17, tbl_18, tbl_19, tbl_20, tbl_21, tbl_22, tbl_23, tbl_24, tbl_25, W_top1, b_top1, W_top2, b_top2, W_top3):
    import jax
    import jax.numpy as jnp

    def _L0_rec_ref(dense_features, sparse_features):
        import jax, jax.numpy as jnp
        import numpy as np
        F = 26
        N = F + 1
        _TRIU_I, _TRIU_J = np.triu_indices(N, k=1)
        combined = jnp.concatenate([dense_features[:, None, :], sparse_features], axis=1)
        interactions = jnp.einsum('bnd,bmd->bnm', combined, combined)
        interactions_flat = interactions[:, _TRIU_I, _TRIU_J]
        return jnp.concatenate([dense_features, interactions_flat], axis=1)
    e = jnp.stack([tbl_0[ids[:, 0]], tbl_1[ids[:, 1]], tbl_2[ids[:, 2]], tbl_3[ids[:, 3]], tbl_4[ids[:, 4]], tbl_5[ids[:, 5]], tbl_6[ids[:, 6]], tbl_7[ids[:, 7]], tbl_8[ids[:, 8]], tbl_9[ids[:, 9]], tbl_10[ids[:, 10]], tbl_11[ids[:, 11]], tbl_12[ids[:, 12]], tbl_13[ids[:, 13]], tbl_14[ids[:, 14]], tbl_15[ids[:, 15]], tbl_16[ids[:, 16]], tbl_17[ids[:, 17]], tbl_18[ids[:, 18]], tbl_19[ids[:, 19]], tbl_20[ids[:, 20]], tbl_21[ids[:, 21]], tbl_22[ids[:, 22]], tbl_23[ids[:, 23]], tbl_24[ids[:, 24]], tbl_25[ids[:, 25]]], axis=1)
    z = _L0_rec_ref(r_dense_features, e)
    z = z.reshape(z.shape[0], -1)
    h = jnp.concatenate([z, r_dense_features], axis=1)
    h = jnp.maximum(h @ W_top1 + b_top1, 0.0)
    h = jnp.maximum(h @ W_top2 + b_top2, 0.0)
    y = h @ W_top3
    return y

_drawn_inputs = setup_inputs


def setup_inputs(seed=0):
    import zlib

    import numpy as np

    out = dict(_drawn_inputs(seed))
    spreads = {'b_top1': (0.0, 0.1), 'b_top2': (0.0, 0.1)}
    factors = {}
    for name, (base, spread) in spreads.items():
        noise = np.random.default_rng([zlib.crc32(name.encode()), seed]).standard_normal(out[name].shape)
        drawn = base * np.exp(spread * noise) if base else spread * noise
        out[name] = jnp.asarray(drawn.astype(out[name].dtype))
    for name, factor in factors.items():
        out[name] = (out[name] * factor).astype(out[name].dtype)
    return out
```

```python
from contextlib import ExitStack

import concourse.bass as bass
from concourse import mybir

F32 = mybir.dt.float32
F32R = mybir.dt.float32r
F16 = mybir.dt.float16
I32 = mybir.dt.int32
U32 = mybir.dt.uint32
ALU = mybir.AluOpType
ACT = mybir.ActivationFunctionType

P = 128
QUAD = 32
ONE_HOT = (0, 2, 4, 6, 7, 8, 9, 11)


def runs(fields):
    out, i = [], 0
    while i < len(fields):
        step = fields[i + 1] - fields[i] if i + 1 < len(fields) else 1
        n = 1
        while i + n < len(fields) and fields[i + n] - fields[i + n - 1] == step:
            n += 1
        out.append((i, fields[i], step, n))
        i += n
    return out


def dlrm_tower(nc, dense, ids, tables, w_top1, b_top1, w_top2, b_top2, w_top3, out):
    B, D = dense.shape
    F = ids.shape[1]
    N = F + 1
    T = B // P
    H1, H2 = w_top1.shape[1], w_top2.shape[1]
    O1, O2 = H1 // P, H2 // P
    M = N - 1
    CH = -(-M // (P // QUAD))
    NQ = P // QUAD
    assert D == P and B == T * P and N <= QUAD

    gathered = [f for f in range(F) if f not in ONE_HOT]
    groups = [gathered[i:i + 4] for i in range(0, len(gathered), 4)]
    NG = len(groups)
    S = len(ONE_HOT)
    TP = [max(p for p in range(1, P + 1) if tables[f].shape[0] % p == 0) for f in ONE_HOT]
    TC = [tables[f].shape[0] // p for f, p in zip(ONE_HOT, TP)]
    assert max(tables[f].shape[0] for f in ONE_HOT) <= 2048
    TPX, TCX = max(TP), max(TC)

    SPAN = 8
    GANGS = P // (4 * SPAN)

    with ExitStack() as ctx:
        def sb(name, shape, dt):
            return ctx.enter_context(nc.sbuf_tensor(name, shape, dt))

        def ps(name, shape, dt):
            return ctx.enter_context(nc.psum_tensor(name, shape, dt))

        def sem(name):
            return ctx.enter_context(nc.semaphore(name))

        ids_i = sb("ids_i", [P, T, F], I32)
        ids_h = sb("ids_h", [P, T, F], F16)
        ident = sb("ident", [P, P], F32)
        ident_h = sb("ident_h", [P, P], F16)
        row_i = sb("row_i", [P, TCX], I32)
        row_of = {tc: sb(f"row_of{tc}", [P, tc], F32) for tc in sorted(set(TC))}
        row_of_i = {tc: sb(f"row_of_i{tc}", [P, tc], I32) for tc in sorted(set(TC))}
        dense_r = sb("dense_r", [P, T, D], F32)
        dense_t = sb("dense_t", [P, B], F32)
        rows = sb("rows", [P, 2, len(gathered), D], F32)
        table = sb("table", [TPX, 2, TCX, D], F32)
        table_hi = sb("table_hi", [TPX, 2, TCX, D], F32R)
        table_lo = sb("table_lo", [TPX, 2, TCX, D], F32R)
        ids_bc = sb("ids_bc", [P, 2, B], F16)
        one_hot = sb("one_hot", [TPX, 2, TCX, B], F32R)
        vecs_t = sb("vecs_t", [P, T, P, QUAD], F32)
        pairs = sb("pairs", [P, CH, B], F32)
        w1_pair = sb("w1_pair", [P, CH, H1], F32)
        w1_d = sb("w1_d", [P, 2, H1], F32)
        w1_dense = sb("w1_dense", [P, H1], F32)
        w2 = sb("w2", [P, O1, H2], F32)
        w3 = sb("w3", [P, O2], F32)
        b1 = sb("b1", [P, O1], F32)
        b2 = sb("b2", [P, O2], F32)
        h1 = sb("h1", [P, O1, B], F32)
        h2 = sb("h2", [P, O2, B], F32)
        y = sb("y", [1, P, T], F32)

        turned = [ps(f"turned{i}", [P, 4, P], F32) for i in range(2)]
        gram = [ps(f"gram{i}", [P, SPAN, P], F32) for i in range(2)]
        acc1 = ps("acc1", [P, O1, P], F32)
        acc2 = ps("acc2", [P, 4, P], F32)

        ids_landed = sem("ids_landed")
        dense_landed = sem("dense_landed")
        table_landed = [sem(f"table_landed{s}") for s in range(S)]
        group_landed = [[sem(f"group_landed{t}_{j}") for j in range(NG)] for t in range(T)]
        w1_landed = sem("w1_landed")
        rest_landed = sem("rest_landed")
        ident_zero = sem("ident_zero")
        ident_ready = sem("ident_ready")
        iota_ready = sem("iota_ready")
        consts_ready = sem("consts_ready")
        pads_ready = sem("pads_ready")
        w1_zero = sem("w1_zero")
        w1_ready = sem("w1_ready")
        ids_spread = sem("ids_spread")
        ids_kept = sem("ids_kept")
        hi_ready = sem("hi_ready")
        lo_ready = sem("lo_ready")
        hot_ready = sem("hot_ready")
        turned_ready = sem("turned_ready")
        kept_act = sem("kept_act")
        kept_dve = sem("kept_dve")
        gram_ready = sem("gram_ready")
        moved_act = sem("moved_act")
        moved_dve = sem("moved_dve")
        acc1_ready = sem("acc1_ready")
        h1_ready = sem("h1_ready")
        acc2_ready = sem("acc2_ready")
        h2_ready = sem("h2_ready")
        y_acc_ready = sem("y_acc_ready")
        y_ready = sem("y_ready")
        out_written = sem("out_written")

        uses = [("dense", None, None)] + [("hot", s, None) for s in range(S)]
        uses += [("group", t, j) for t in range(T) for j in range(NG)]
        number = {u: n for n, u in enumerate(uses)}
        by_act = [u[0] != "group" or n % 2 == 0 for n, u in enumerate(uses)]
        kept = {}
        for n, u in enumerate(uses):
            same = by_act[:n + 1].count(by_act[n])
            kept[n] = (kept_act if by_act[n] else kept_dve, same)

        def vec_slots(t, n, step, count):
            v = vecs_t[:, t].rearrange("d b n -> d n b")
            return v[:, n:n + step * (count - 1) + 1:step, :]

        def gram_block(s, q, w, g):
            col = s * M + q * CH
            return gram[g % 2][QUAD * s:QUAD * s + QUAD, :, col:col + w].rearrange("n k c -> n c k")

        def pair_place(s, q, w, g):
            b = g * SPAN * 4
            return pairs[QUAD * q:QUAD * q + QUAD, 0:w, b + s:b + 4 * SPAN:4]

        block = ctx.enter_context(nc.Block())

        @block.sync
        def _(sp):
            sp.dma_start(ids_i[:], ids.rearrange("(p t) f -> p t f", t=T)).then_inc(ids_landed, 16)
            sp.dma_start(dense_r[:], dense.rearrange("(p t) d -> p t d", t=T)).then_inc(dense_landed, 16)

            def load_table(s):
                src = tables[ONE_HOT[s]].rearrange("(p c) d -> p c d", c=TC[s])
                cut = TP[s] // 16 * 16
                if s >= 2:
                    sp.wait_ge(hi_ready, s - 1)
                    sp.wait_ge(lo_ready, s - 1)
                sp.dma_start(table[0:cut, s % 2, 0:TC[s], :], src[0:cut]).then_inc(table_landed[s], 16)
                sp.dma_start(table[cut:TP[s], s % 2, 0:TC[s], :], src[cut:TP[s]]).then_inc(table_landed[s], 16)

            load_table(0)
            load_table(1)
            for s in range(2, S):
                load_table(s)
            sp.wait_ge(w1_zero, 1)
            for m in range(M):
                q, c = divmod(m, CH)
                first = D + m * N - m * (m + 1) // 2
                sp.dma_start(w1_pair[QUAD * q + m + 1:QUAD * q + N, c, :],
                             w_top1[first:first + N - 1 - m, :]).then_inc(w1_landed, 16)
            sp.dma_start(w1_d[:, 0, :], w_top1[0:D, :]).then_inc(w1_landed, 16)
            sp.dma_start(w1_d[:, 1, :], w_top1[w_top1.shape[0] - D:, :]).then_inc(w1_landed, 16)
            sp.dma_start(w2[:], w_top2.rearrange("(c p) n -> p c n", p=P)).then_inc(rest_landed, 16)
            with nc.allow_non_contiguous_dma(reason="biases and a column, one element per partition"):
                sp.dma_start(b1[:], b_top1.rearrange("(c p) -> p c", p=P)).then_inc(rest_landed, 16)
                sp.dma_start(b2[:], b_top2.rearrange("(c p) -> p c", p=P)).then_inc(rest_landed, 16)
                sp.dma_start(w3[:], w_top3.rearrange("(c p) o -> p (c o)", p=P)).then_inc(rest_landed, 16)
            sp.wait_ge(y_ready, T)
            sp.dma_start(out.rearrange("(a b) o -> a (b o)", a=1),
                         y[:].rearrange("a p t -> a (p t)")).then_inc(out_written, 16)
            sp.wait_ge(out_written, 16)

        @block.gpsimd
        def _(pool):
            pool.memset(ident[:], 0.0).then_inc(ident_zero, 1)
            pool.wait_ge(ident_zero, 1)
            pool.affine_select(out=ident[:], in_=ident[:], compare_op=ALU.not_equal, fill=1.0, base=0,
                               pattern=[[-1, P]], channel_multiplier=1).then_inc(ident_ready, 1)
            for tc in sorted(row_of):
                pool.iota(row_of_i[tc][:], pattern=[[1, tc]], base=0, channel_multiplier=tc).then_inc(iota_ready, 1)
            pool.wait_ge(ids_landed, 16)
            at = {f: i for i, f in enumerate(gathered)}
            for t in range(T):
                for j, group in enumerate(groups):
                    if t >= 2:
                        pool.wait_ge(turned_ready, number["group", t - 2, j] + 1)
                    for f in group:
                        pool.indirect_dma_start(
                            rows[:, t % 2, at[f], :], None, tables[f],
                            bass.IndirectOffsetOnAxis(ap=ids_i[:, t, f:f + 1].bitcast(U32), axis=0),
                        ).then_inc(group_landed[t][j], 16)

        @block.vector
        def _(dve):
            nc.vector.memset(w1_pair[:], 0.0).then_inc(w1_zero, 1)
            nc.vector.memset(vecs_t[:, :, :, N:QUAD], 0.0).then_inc(pads_ready, 1)
            dve.wait_ge(iota_ready, len(row_of))
            for tc in sorted(row_of):
                nc.vector.tensor_copy(row_of[tc][:], row_of_i[tc][:])
            dve.wait_ge(ident_ready, 1)
            nc.vector.tensor_copy(ident_h[:], ident[:])
            dve.wait_ge(ids_landed, 16)
            nc.vector.tensor_scalar(ids_h[:], ids_i[:], 2047.0, None, ALU.min).then_inc(consts_ready, 1)
            dve.wait_ge(consts_ready, 1)
            for s in range(S):
                dve.wait_ge(ids_kept, s + 1)
                if s >= 2:
                    dve.wait_ge(turned_ready, number["hot", s - 2, None] + 1)
                for c in range(TC[s]):
                    nc.vector.tensor_scalar(one_hot[0:TP[s], s % 2, c, :], ids_bc[0:TP[s], s % 2, :],
                                            row_of[TC[s]][0:TP[s], c:c + 1], None,
                                            ALU.is_equal).then_inc(hot_ready, 1)
                    if c == 0:
                        dve.wait_ge(hi_ready, s + 1)
                        nc.vector.tensor_tensor(table_lo[0:TP[s], s % 2, 0:TC[s], :],
                                                table[0:TP[s], s % 2, 0:TC[s], :],
                                                table_hi[0:TP[s], s % 2, 0:TC[s], :],
                                                ALU.subtract).then_inc(lo_ready, 1)
            dve.wait_ge(w1_landed, 16 * (M + 2))
            nc.vector.tensor_tensor(w1_dense[:], w1_d[:, 0, :], w1_d[:, 1, :], ALU.add).then_inc(w1_ready, 1)
            for t in range(T):
                for j in range(NG):
                    n = number["group", t, j]
                    if not by_act[n]:
                        dve.wait_ge(turned_ready, n + 1)
                        for at, f, step, count in runs(groups[j]):
                            last = nc.vector.tensor_copy(vec_slots(t, f + 1, step, count),
                                                         turned[n % 2][:, at:at + count, :])
                        last.then_inc(kept_dve, 1)
                for k in range(GANGS):
                    g = GANGS * t + k
                    dve.wait_ge(gram_ready, g + 1)
                    for s in (2, 3):
                        for q in range(NQ):
                            w = min(CH, M - CH * q)
                            last = nc.vector.tensor_copy(pair_place(s, q, w, g), gram_block(s, q, w, g))
                    last.then_inc(moved_dve, 1)

        @block.scalar
        def _(act):
            def keep(n):
                kind, a, j = uses[n]
                act.wait_ge(turned_ready, n + 1)
                if kind == "dense":
                    for t in range(T):
                        nc.scalar.activation(vec_slots(t, 0, 1, 1), turned[n % 2][:, t:t + 1, :], ACT.Copy)
                    last = nc.scalar.activation(dense_t[:].rearrange("d (t b) -> d t b", t=T), turned[n % 2][:], ACT.Copy)
                elif kind == "hot":
                    v = vecs_t[:, :, :, ONE_HOT[a] + 1]
                    last = nc.scalar.activation(v, turned[n % 2][:], ACT.Copy)
                else:
                    for at, f, step, count in runs(groups[j]):
                        last = nc.scalar.activation(vec_slots(a, f + 1, step, count),
                                                    turned[n % 2][:, at:at + count, :], ACT.Copy)
                last.then_inc(kept_act, 1)

            keep(0)
            for s in range(S):
                act.wait_ge(ids_spread, s + 1)
                if s >= 2:
                    act.wait_ge(hot_ready, sum(TC[:s - 1]))
                nc.scalar.activation(ids_bc[:, s % 2, :], acc2[:], ACT.Copy).then_inc(ids_kept, 1)
                act.wait_ge(table_landed[s], 32)
                if s >= 2:
                    act.wait_ge(turned_ready, number["hot", s - 2, None] + 1)
                nc.scalar.activation(table_hi[0:TP[s], s % 2, 0:TC[s], :], table[0:TP[s], s % 2, 0:TC[s], :],
                                     ACT.Copy).then_inc(hi_ready, 1)
                if s:
                    keep(number["hot", s - 1, None])
            keep(number["hot", S - 1, None])

            def layers_end(t):
                b = slice(t * P, t * P + P)
                act.wait_ge(acc1_ready, t + 1)
                for o in range(O1):
                    last = nc.scalar.activation(h1[:, o, b], acc1[:, o, :], ACT.Relu, bias=b1[:, o:o + 1])
                last.then_inc(h1_ready, 1)
                act.wait_ge(acc2_ready, t + 1)
                for o in range(O2):
                    last = nc.scalar.activation(h2[:, o, b], acc2[:, o, :], ACT.Relu, bias=b2[:, o:o + 1])
                last.then_inc(h2_ready, 1)
                act.wait_ge(y_acc_ready, t + 1)
                nc.scalar.activation(y[0:1, :, t], acc2[0:1, O2, :], ACT.Copy).then_inc(y_ready, 1)

            act.wait_ge(rest_landed, 64)
            for t in range(T):
                for j in range(NG):
                    n = number["group", t, j]
                    if by_act[n]:
                        keep(n)
                for k in range(GANGS):
                    g = GANGS * t + k
                    act.wait_ge(gram_ready, g + 1)
                    for s in (0, 1):
                        for q in range(NQ):
                            w = min(CH, M - CH * q)
                            last = nc.scalar.activation(pair_place(s, q, w, g), gram_block(s, q, w, g), ACT.Copy)
                    last.then_inc(moved_act, 1)
                layers_end(t)

        @block.tensor
        def _(pe):
            def bank_free(n):
                if n >= 2:
                    pe.wait_ge(*kept[n - 2])

            pe.wait_ge(ident_ready, 1)
            pe.wait_ge(dense_landed, 16)
            for t in range(T):
                last = nc.tensor.transpose(turned[0][:, t, :], dense_r[:, t, :], ident[:])
            last.then_inc(turned_ready, 1)

            def spread_ids(s):
                if s:
                    pe.wait_ge(ids_kept, s)
                for t in range(T):
                    col = ids_h[:, t, ONE_HOT[s]:ONE_HOT[s] + 1]
                    last = nc.tensor.matmul(acc2[:, t, :], col.to_broadcast([P, P]), ident_h[:], start=True, stop=True)
                last.then_inc(ids_spread, 1)

            pe.wait_ge(consts_ready, 1)
            spread_ids(0)
            for s in range(S):
                if s + 1 < S:
                    spread_ids(s + 1)
                n = number["hot", s, None]
                bank_free(n)
                for c in range(TC[s]):
                    pe.wait_ge(hot_ready, sum(TC[:s]) + c + 1)
                    if c == 0:
                        pe.wait_ge(lo_ready, s + 1)
                    for part in (table_hi, table_lo):
                        last = nc.tensor.matmul(turned[n % 2][:], part[0:TP[s], s % 2, c, :],
                                                one_hot[0:TP[s], s % 2, c, :],
                                                start=(c == 0 and part is table_hi),
                                                stop=(c == TC[s] - 1 and part is table_lo))
                last.then_inc(turned_ready, 1)

            at = {f: i for i, f in enumerate(gathered)}
            for t in range(T):
                b = slice(t * P, t * P + P)
                for j, group in enumerate(groups):
                    n = number["group", t, j]
                    bank_free(n)
                    pe.wait_ge(group_landed[t][j], 16 * len(group))
                    for i, f in enumerate(group):
                        last = nc.tensor.transpose(turned[n % 2][:, i, :], rows[:, t % 2, at[f], :], ident[:])
                    last.then_inc(turned_ready, 1)
                n = number["group", t, NG - 1]
                pe.wait_ge(*kept[n])
                pe.wait_ge(*kept[n - 1])
                if t == 0:
                    pe.wait_ge(kept_act, S + 1)
                    pe.wait_ge(pads_ready, 1)
                for k in range(GANGS):
                    g = GANGS * t + k
                    if g >= 2:
                        pe.wait_ge(moved_act, g - 1)
                        pe.wait_ge(moved_dve, g - 1)
                    for i in range(SPAN):
                        first = (k * SPAN + i) * 4
                        four = vecs_t[:, t, first:first + 4, :]
                        last = nc.tensor.matmul(gram[g % 2][:, i, 0:4 * M].rearrange("n (s m) -> n s m", m=M),
                                                four.rearrange("d s n -> d (s n)"), four[:, :, 0:M],
                                                start=True, stop=True)
                    last.then_inc(gram_ready, 1)
                if t == 0:
                    pe.wait_ge(w1_ready, 1)
                    pe.wait_ge(rest_landed, 64)
                else:
                    pe.wait_ge(h1_ready, t)
                pe.wait_ge(moved_act, GANGS * (t + 1))
                pe.wait_ge(moved_dve, GANGS * (t + 1))
                for o in range(O1):
                    oc = slice(o * P, o * P + P)
                    nc.tensor.matmul(acc1[:, o, :], w1_dense[:, oc], dense_t[:, b], start=True, stop=False)
                    for c in range(CH):
                        k = P if CH * (NQ - 1) + c < M else P - QUAD
                        last = nc.tensor.matmul(acc1[:, o, :], w1_pair[0:k, c, oc], pairs[0:k, c, b],
                                                start=False, stop=(c == CH - 1))
                last.then_inc(acc1_ready, 1)
                pe.wait_ge(h1_ready, t + 1)
                if t:
                    pe.wait_ge(y_ready, t)
                for o in range(O2):
                    for c in range(O1):
                        last = nc.tensor.matmul(acc2[:, o, :], w2[:, c, o * P:o * P + P], h1[:, c, b],
                                                start=(c == 0), stop=(c == O1 - 1))
                last.then_inc(acc2_ready, 1)
                pe.wait_ge(h2_ready, t + 1)
                for c in range(O2):
                    last = nc.tensor.matmul(acc2[0:1, O2, :], w3[:, c:c + 1], h2[:, c, b],
                                            start=(c == 0), stop=(c == O2 - 1))
                last.then_inc(y_acc_ready, 1)


def kernel(**inputs):
    import numpy as _np
    import concourse.bacc as _bacc
    from concourse import mybir as _mybir
    from concourse.bass_utils import run_bass_kernel_spmd as _run

    nc = _bacc.Bacc("TRN2", target_bir_lowering=False, num_devices=1)
    arrays, aps = {}, {}
    for name, value in inputs.items():
        a = _np.ascontiguousarray(value)
        arrays[f"in_{name}"] = a
        aps[name] = nc.dram_tensor(f"in_{name}", a.shape, _mybir.dt.from_np(a.dtype), kind="ExternalInput").ap()
    batch, fields = arrays["in_ids"].shape
    out = nc.dram_tensor("out_y", (batch, 1), _mybir.dt.float32, kind="ExternalOutput").ap()
    dlrm_tower(nc, aps["r_dense_features"], aps["ids"], [aps[f"tbl_{f}"] for f in range(fields)],
               aps["W_top1"], aps["b_top1"], aps["W_top2"], aps["b_top2"], aps["W_top3"], out)
    r = _run(nc, [arrays], core_ids=[0])
    return r.results[0]["out_y"]
```

```python
from contextlib import ExitStack

import concourse.bass as bass
from concourse import mybir

F32 = mybir.dt.float32
F32R = mybir.dt.float32r
F16 = mybir.dt.float16
I32 = mybir.dt.int32
U32 = mybir.dt.uint32
ALU = mybir.AluOpType
ACT = mybir.ActivationFunctionType

P = 128
QUAD = 32
ONE_HOT = (0, 2, 4, 6, 7, 8, 9)


def runs(fields):
    out, i = [], 0
    while i < len(fields):
        step = fields[i + 1] - fields[i] if i + 1 < len(fields) else 1
        n = 1
        while i + n < len(fields) and fields[i + n] - fields[i + n - 1] == step:
            n += 1
        out.append((i, fields[i], step, n))
        i += n
    return out


def dlrm_tower(nc, dense, ids, tables, w_top1, b_top1, w_top2, b_top2, w_top3, out):
    B, D = dense.shape
    F = ids.shape[1]
    N = F + 1
    T = B // P
    H1, H2 = w_top1.shape[1], w_top2.shape[1]
    O1, O2 = H1 // P, H2 // P
    M = N - 1
    CH = -(-M // (P // QUAD))
    NQ = P // QUAD
    assert D == P and B == T * P and N <= QUAD

    gathered = [f for f in range(F) if f not in ONE_HOT]
    groups = [gathered[i:i + 4] for i in range(0, len(gathered), 4)]
    NG = len(groups)
    S = len(ONE_HOT)
    TP = [max(p for p in range(1, P + 1) if tables[f].shape[0] % p == 0) for f in ONE_HOT]
    TC = [tables[f].shape[0] // p for f, p in zip(ONE_HOT, TP)]
    assert max(tables[f].shape[0] for f in ONE_HOT) <= 2048
    TPX, TCX = max(TP), max(TC)
    BY_ACT = [1] * S

    C1 = CH + 1
    BATCHES = ((0, T - 2), (T - 2, T - 1), (T - 1, T))
    assert T == 4
    BW = max(b - a for a, b in BATCHES) * P
    HALF = P // 2

    WARM = 5
    SPAN = 8
    GANGS = P // (4 * SPAN)

    with ExitStack() as ctx:
        def sb(name, shape, dt):
            return ctx.enter_context(nc.sbuf_tensor(name, shape, dt))

        def ps(name, shape, dt):
            return ctx.enter_context(nc.psum_tensor(name, shape, dt))

        def sem(name):
            return ctx.enter_context(nc.semaphore(name))

        ids_i = sb("ids_i", [P, T, F], I32)
        ids_h = sb("ids_h", [P, T, F], F16)
        ident = sb("ident", [P, P], F32)
        ident_h = sb("ident_h", [P, P], F16)
        row_i = sb("row_i", [P, TCX], I32)
        row_of = {tc: sb(f"row_of{tc}", [P, tc], F32) for tc in sorted(set(TC))}
        row_of_i = {tc: sb(f"row_of_i{tc}", [P, tc], I32) for tc in sorted(set(TC))}
        dense_r = sb("dense_r", [P, T, D], F32)
        dense_t = sb("dense_t", [P, B], F32)
        dense_hi = sb("dense_hi", [P, BW], F32R)
        dense_lo = sb("dense_lo", [P, BW], F32R)
        rows = sb("rows", [P, 2, len(gathered), D], F32)
        table = sb("table", [TPX, 2, TCX, D], F32)
        table_hi = sb("table_hi", [TPX, 2, TCX, D], F32R)
        table_lo = sb("table_lo", [TPX, 2, TCX, D], F32R)
        ids_bc = sb("ids_bc", [P, 2, B], F32)
        one_hot = sb("one_hot", [P, 2, TCX, B], F32R)
        assert B == H1 and TCX == C1 and O2 == 2
        w1_hi, w1_lo = one_hot[:, S % 2], one_hot[:, (S - 1) % 2]
        vecs_t = sb("vecs_t", [P, T, P, QUAD], F32)
        pairs = sb("pairs", [P, CH, P], F32)
        pairs_hi = sb("pairs_hi", [P, CH, BW], F32R)
        pairs_lo = sb("pairs_lo", [P, CH, BW], F32R)
        w1 = sb("w1", [P, C1, H1], F32)
        w1_last = sb("w1_last", [P, H1], F32)
        w2 = sb("w2", [P, O1, H2], F32)
        w3 = sb("w3", [P, O2], F32)
        b1 = sb("b1", [P, O1], F32)
        b2 = sb("b2", [P, O2], F32)
        h1 = sb("h1", [P, O1, BW], F32)
        square = h1[:].rearrange("p o b -> p (o b)")[:, 0:B]
        h2 = ids_bc[:, :, 0:BW]
        y = sb("y", [1, P, T], F32)

        turned = [ps(f"turned{i}", [P, 4, P], F32) for i in range(2)]
        gram = [ps(f"gram{i}", [P, SPAN, P], F32) for i in range(2)]
        acc = [ps(f"acc{i}", [P, B], F32) for i in range(2)]

        ids_landed = sem("ids_landed")
        dense_landed = sem("dense_landed")
        table_landed = [sem(f"table_landed{s}") for s in range(S)]
        group_landed = [[sem(f"group_landed{t}_{j}") for j in range(NG)] for t in range(T)]
        w1_landed = sem("w1_landed")
        rest_landed = sem("rest_landed")
        ident_zero = sem("ident_zero")
        ident_ready = sem("ident_ready")
        iota_ready = sem("iota_ready")
        consts_ready = sem("consts_ready")
        pairs_zero = sem("pairs_zero")
        pads_ready = sem("pads_ready")
        w1_zero = sem("w1_zero")
        w1_ready = sem("w1_ready")
        acc_ready = sem("acc_ready")
        acc_kept = sem("acc_kept")
        hi_ready = sem("hi_ready")
        lo_ready = sem("lo_ready")
        hot_ready = sem("hot_ready")
        hot_square = sem("hot_square")
        hot_ready_act = sem("hot_ready_act")
        turned_ready = sem("turned_ready")
        kept_act = sem("kept_act")
        kept_dve = sem("kept_dve")
        gram_ready = sem("gram_ready")
        moved_act = sem("moved_act")
        moved_dve = sem("moved_dve")
        pairs_hi_ready = sem("pairs_hi_ready")
        pairs_split = sem("pairs_split")
        w1_hi_ready = sem("w1_hi_ready")
        w1_lo_ready = sem("w1_lo_ready")
        dense_split = sem("dense_split")
        out_written = sem("out_written")

        EARLY = {S - NG + 1 + j: (j,) for j in range(NG - 2)} | {S - 1: (NG - 2, NG - 1)}
        uses = [("dense", None, None)]
        for s in range(S):
            uses += [("group", 0, j) for j in EARLY.get(s, ())] + [("hot", s, None)]
        uses += [("group", t, j) for t in range(1, T) for j in range(NG)]
        number = {u: n for n, u in enumerate(uses)}
        by_act = [u[0] != "group" or u[1:] < (T - 1, 0) or n % 2 == 0 for n, u in enumerate(uses)]
        kept = {}
        for n, u in enumerate(uses):
            same = by_act[:n + 1].count(by_act[n])
            kept[n] = (kept_act if by_act[n] else kept_dve, same)

        acc_uses = [("ids", s, None) for s in range(S)]
        for a in range(len(BATCHES)):
            acc_uses += [("one", a, o) for o in range(O1)] + [("two", a, o) for o in range(O2)] + [("three", a, 0)]
        acc_number = {u: n for n, u in enumerate(acc_uses)}

        layers = [[u for u in acc_uses if u[1] == a and u[0] != "ids"] for a in range(len(BATCHES))]
        def woven(blocks, turns):
            out = []
            for i in range(max(len(blocks), len(turns))):
                out += blocks[i:i + 1] + turns[i:i + 1]
            return out

        grams = [[("gram", t, k) for k in range(GANGS)] for t in range(T)]
        turns = [[("turn", t, j) for j in range(NG)] for t in range(T)]
        blocks = [[u for u in acc_uses if u[1] == a and u[0] != "ids"] for a in range(len(BATCHES))]
        steps = []
        splits = []
        for t in range(T - 2):
            for k in range(GANGS):
                steps.append(grams[t][k])
                if t == 0:
                    steps += [turn for j, turn in enumerate(turns[1]) if min(GANGS - 2, j * (GANGS - 1) // NG) == k]
                steps += splits
                splits = [("split", t, k // 2)] if k % 2 else []
                if (t, k) == (1, 0):
                    steps.append(("parts", 0, None))
        steps += splits + turns[2][0:2]
        for o, u in enumerate(blocks[0]):
            if o + 1 < O1:
                steps.append(("parts", o + 1, None))
            steps.append(u)
            steps += turns[2][2 + o:3 + o]
        steps += grams[2] + turns[3][0:2] + woven(blocks[1], turns[3][2:])
        steps += grams[3] + blocks[2]
        assert sorted(x for x in steps if x[0] == "turn") == sum(turns[1:], [])

        def bank_key(n):
            kind, t, j = uses[n]
            if (kind, t) == ("group", 0):
                return 1, j % 4
            return 0, sum(u[:2] != ("group", 0) for u in uses[:n]) % 2

        def bank(n):
            which, i = bank_key(n)
            return gram[i // 2][:, i % 2 * 4:i % 2 * 4 + 4, :] if which else turned[i][:]

        def vec_slots(t, n, step, count):
            v = vecs_t[:, t].rearrange("d b n -> d n b")
            return v[:, n:n + step * (count - 1) + 1:step, :]

        def gram_block(s, q, w, g):
            col = s * M + q * CH
            return gram[g % 2][QUAD * s:QUAD * s + QUAD, :, col:col + w].rearrange("n k c -> n c k")

        def pair_place(s, q, w, g):
            b = g % GANGS * SPAN * 4
            return pairs[QUAD * q:QUAD * q + QUAD, 0:w, b + s:b + 4 * SPAN:4]

        def hot_by_dve(s):
            return sum(TC[:s]) - sum(BY_ACT[:s])

        block = ctx.enter_context(nc.Block())

        @block.sync
        def _(sp):
            sp.dma_start(ids_i[:], ids.rearrange("(p t) f -> p t f", t=T)).then_inc(ids_landed, 16)

            def load_table(s):
                src = tables[ONE_HOT[s]].rearrange("(p c) d -> p c d", c=TC[s])
                cut = TP[s] // 16 * 16
                if s >= 2:
                    sp.wait_ge(hi_ready, s - 1)
                    sp.wait_ge(lo_ready, s - 1)
                sp.dma_start(table[0:cut, s % 2, 0:TC[s], :], src[0:cut]).then_inc(table_landed[s], 16)
                sp.dma_start(table[cut:TP[s], s % 2, 0:TC[s], :], src[cut:TP[s]]).then_inc(table_landed[s], 16)

            def load_w1(m):
                q, c = divmod(m, CH)
                first = D + m * N - m * (m + 1) // 2
                sp.dma_start(w1[QUAD * q + m + 1:QUAD * q + N, c, :],
                             w_top1[first:first + N - 1 - m, :]).then_inc(w1_landed, 16)

            load_table(0)
            sp.dma_start(dense_r[:], dense.rearrange("(p t) d -> p t d", t=T)).then_inc(dense_landed, 16)
            load_table(1)
            sp.wait_ge(pairs_zero, 1)
            sp.dma_start(w1[:, 0:CH, :], pairs[:, 0:H1 // P, :].rearrange("p (a c) b -> p a (c b)", a=1)
                         .to_broadcast([P, CH, H1])).then_inc(w1_zero, 16)
            load_table(2)
            per = -(-M // (S - 3))
            for s in range(3, S):
                load_table(s)
                if s == 3:
                    sp.wait_ge(w1_zero, 16)
                for m in range(per * (s - 3), min(M, per * (s - 2))):
                    load_w1(m)
            sp.dma_start(w1[:, CH, :], w_top1[0:D, :]).then_inc(w1_landed, 16)
            sp.dma_start(w1_last[:], w_top1[w_top1.shape[0] - D:, :]).then_inc(w1_landed, 16)
            sp.dma_start(w2[:], w_top2.rearrange("(c p) n -> p c n", p=P)).then_inc(rest_landed, 16)
            with nc.allow_non_contiguous_dma(reason="biases and a column, one element per partition"):
                sp.dma_start(b1[:], b_top1.rearrange("(c p) -> p c", p=P)).then_inc(rest_landed, 16)
                sp.dma_start(b2[:], b_top2.rearrange("(c p) -> p c", p=P)).then_inc(rest_landed, 16)
                sp.dma_start(w3[:], w_top3.rearrange("(c p) o -> p (c o)", p=P)).then_inc(rest_landed, 16)
            sp.wait_ge(acc_kept, len(acc_uses))
            sp.dma_start(out.rearrange("(a b) o -> a (b o)", a=1),
                         y[:].rearrange("a p t -> a (p t)")).then_inc(out_written, 16)
            sp.wait_ge(out_written, 16)

        @block.gpsimd
        def _(pool):
            pool.memset(ident[:], 0.0).then_inc(ident_zero, 1)
            pool.wait_ge(ident_zero, 1)
            pool.affine_select(out=ident[:], in_=ident[:], compare_op=ALU.not_equal, fill=1.0, base=0,
                               pattern=[[-1, P]], channel_multiplier=1).then_inc(ident_ready, 1)
            for tc in sorted(row_of):
                pool.iota(row_of_i[tc][:], pattern=[[1, tc]], base=0, channel_multiplier=tc).then_inc(iota_ready, 1)
            pool.wait_ge(ids_landed, 16)
            at = {f: i for i, f in enumerate(gathered)}
            for t in range(T):
                for j, group in enumerate(groups):
                    if t >= 2:
                        pool.wait_ge(turned_ready, number["group", t - 2, j] + 1)
                    for f in group:
                        pool.indirect_dma_start(
                            rows[:, t % 2, at[f], :], None, tables[f],
                            bass.IndirectOffsetOnAxis(ap=ids_i[:, t, f:f + 1].bitcast(U32), axis=0),
                        ).then_inc(group_landed[t][j], 16)

        @block.vector
        def _(dve):
            nc.vector.memset(pairs[:], 0.0).then_inc(pairs_zero, 1)
            dve.wait_ge(iota_ready, len(row_of))
            for tc in sorted(row_of):
                nc.vector.tensor_copy(row_of[tc][:], row_of_i[tc][:])
            dve.wait_ge(ident_ready, 1)
            nc.vector.tensor_copy(ident_h[:], ident[:])
            dve.wait_ge(ids_landed, 16)
            nc.vector.tensor_scalar(ids_h[:], ids_i[:], 2047.0, None, ALU.min).then_inc(consts_ready, 1)
            dve.wait_ge(consts_ready, 1)
            for s in range(S):
                dve.wait_ge(acc_kept, s + 1)
                if s >= 2:
                    dve.wait_ge(turned_ready, number["hot", s - 2, None] + 1)
                for c in range(TC[s] - BY_ACT[s]):
                    nc.vector.tensor_scalar(one_hot[0:TP[s], s % 2, c, :], ids_bc[0:TP[s], s % 2, :],
                                            row_of[TC[s]][0:TP[s], c:c + 1], None,
                                            ALU.is_equal).then_inc(hot_ready, 1)
                    if c == 3:
                        dve.wait_ge(hi_ready, s + 1)
                        nc.vector.tensor_tensor(table_lo[0:TP[s], s % 2, 0:TC[s], :],
                                                table[0:TP[s], s % 2, 0:TC[s], :],
                                                table_hi[0:TP[s], s % 2, 0:TC[s], :],
                                                ALU.subtract).then_inc(lo_ready, 1)
            dve.wait_ge(kept_act, 1)
            nc.vector.tensor_copy(dense_hi[:], dense_t[:, 0:BW]).then_inc(dense_split, 1)
            dve.wait_ge(dense_split, 1)
            nc.vector.tensor_tensor(dense_lo[:], dense_t[:, 0:BW], dense_hi[:], ALU.subtract).then_inc(dense_split, 1)

            dve.wait_ge(w1_landed, 16 * (M + 2))
            nc.vector.tensor_tensor(w1[:, CH, :], w1[:, CH, :], w1_last[:], ALU.add).then_inc(w1_ready, 1)

            def split_pairs(t, half):
                src = pairs[:, :, half * HALF:half * HALF + HALF]
                at = t * P + half * HALF
                hi, lo = pairs_hi[:, :, at:at + HALF], pairs_lo[:, :, at:at + HALF]
                dve.wait_ge(moved_act, GANGS * t + 2 * half + 2)
                dve.wait_ge(moved_dve, GANGS * t + 2 * half + 2)
                nc.vector.tensor_copy(hi, src).then_inc(pairs_hi_ready, 1)
                dve.wait_ge(pairs_hi_ready, 2 * t + half + 1)
                nc.vector.tensor_tensor(lo, src, hi, ALU.subtract).then_inc(pairs_split, 1)

            def turned_kept(t, j):
                n = number["group", t, j]
                if not by_act[n]:
                    dve.wait_ge(turned_ready, n + 1)
                    for at, f, step, count in runs(groups[j]):
                        last = nc.vector.tensor_copy(vec_slots(t, f + 1, step, count),
                                                     bank(n)[:, at:at + count, :])
                    last.then_inc(kept_dve, 1)

            def pairs_moved(t, k):
                g = GANGS * t + k
                dve.wait_ge(gram_ready, g + 1)
                if k % 2 == 0 and 0 < t < T - 1:
                    dve.wait_ge(pairs_split, 2 * (t - 1) + k // 2 + 1)
                if k == 0 and t == T - 1:
                    dve.wait_ge(acc_ready, acc_number["one", 1, O1 - 1] + 1)
                for s in (2, 3):
                    for q in range(NQ):
                        w = min(CH, M - CH * q)
                        last = nc.vector.tensor_copy(pair_place(s, q, w, g), gram_block(s, q, w, g))
                last.then_inc(moved_dve, 1)

            def weights_low(o):
                dve.wait_ge(w1_hi_ready, o + 1)
                if o == 0:
                    dve.wait_ge(turned_ready, number["hot", S - 1, None] + 1)
                oc = slice(o * P, o * P + P)
                nc.vector.tensor_tensor(w1_lo[:, :, oc], w1[:, :, oc], w1_hi[:, :, oc],
                                        ALU.subtract).then_inc(w1_lo_ready, 1)

            for kind, a, i in steps:
                if kind == "turn":
                    turned_kept(a, i)
                elif kind == "gram":
                    pairs_moved(a, i)
                elif kind == "split":
                    split_pairs(a, i)
                elif kind == "parts":
                    weights_low(a)

        @block.scalar
        def _(act):
            def keep(n):
                kind, a, j = uses[n]
                act.wait_ge(turned_ready, n + 1)
                if kind == "dense":
                    for t in range(T):
                        nc.scalar.activation(vec_slots(t, 0, 1, 1), bank(n)[:, t:t + 1, :], ACT.Copy)
                    last = nc.scalar.activation(dense_t[:].rearrange("d (t b) -> d t b", t=T), bank(n), ACT.Copy)
                elif kind == "hot":
                    v = vecs_t[:, :, :, ONE_HOT[a] + 1]
                    last = nc.scalar.activation(v, bank(n), ACT.Copy)
                else:
                    for at, f, step, count in runs(groups[j]):
                        last = nc.scalar.activation(vec_slots(a, f + 1, step, count),
                                                    bank(n)[:, at:at + count, :], ACT.Copy)
                last.then_inc(kept_act, 1)

            def spread_kept(s):
                act.wait_ge(acc_ready, s + 1)
                if s >= 2:
                    act.wait_ge(hot_ready, hot_by_dve(s - 1))
                nc.scalar.activation(ids_bc[:, s % 2, :], acc[s % 2][:], ACT.Copy).then_inc(acc_kept, 1)

            def hots_last(s):
                act.wait_ge(acc_kept, s + 1)
                if s == 0:
                    act.wait_ge(consts_ready, 1)
                if s >= 2:
                    act.wait_ge(turned_ready, number["hot", s - 2, None] + 1)
                for c in range(TC[s] - BY_ACT[s], TC[s]):
                    made = sum(BY_ACT[:s]) + c - (TC[s] - BY_ACT[s])
                    if made:
                        act.wait_ge(hot_ready_act, made)
                    nc.scalar.activation(square[0:TP[s], :], ids_bc[0:TP[s], s % 2, :], ACT.Square, scale=-1.0,
                                         bias=row_of[TC[s]][0:TP[s], c:c + 1]).then_inc(hot_square, 1)
                    act.wait_ge(hot_square, made + 1)
                    nc.scalar.activation(one_hot[0:TP[s], s % 2, c, :], square[0:TP[s], :], ACT.Relu,
                                         scale=-1.0, bias=1.0).then_inc(hot_ready_act, 1)

            def table_high(s):
                act.wait_ge(table_landed[s], 32)
                if s >= 2:
                    act.wait_ge(turned_ready, number["hot", s - 2, None] + 1)
                nc.scalar.activation(table_hi[0:TP[s], s % 2, 0:TC[s], :], table[0:TP[s], s % 2, 0:TC[s], :],
                                     ACT.Copy).then_inc(hi_ready, 1)

            spread_kept(0)
            table_high(0)
            hots_last(0)
            keep(0)
            spread_kept(1)
            table_high(1)
            hots_last(1)
            act.wait_ge(ident_ready, 1)

            def pads(t):
                zero = ident[:].rearrange("p (a b) -> p a b", a=1).to_broadcast([P, QUAD - N, P])
                nc.scalar.activation(vecs_t[:, t, :, N:QUAD].rearrange("d b n -> d n b"), zero,
                                     ACT.Copy, scale=0.0).then_inc(pads_ready, 1)

            for s in range(1, S):
                if s + 1 < S:
                    spread_kept(s + 1)
                keep(number["hot", s - 1, None])
                for j in EARLY.get(s, ()):
                    keep(number["group", 0, j])
                if s + 1 < S:
                    table_high(s + 1)
                    hots_last(s + 1)
                if s <= 2:
                    pads(s - 1)
            keep(number["hot", S - 1, None])

            def layer_kept(kind, batch, o):
                n = acc_number[kind, batch, o]
                first, end = BATCHES[batch]
                w = (end - first) * P
                act.wait_ge(acc_ready, n + 1)
                if kind == "one":
                    last = nc.scalar.activation(h1[:, o, 0:w], acc[n % 2][:, 0:w], ACT.Relu, bias=b1[:, o:o + 1])
                elif kind == "two":
                    last = nc.scalar.activation(h2[:, o, 0:w], acc[n % 2][:, 0:w], ACT.Relu, bias=b2[:, o:o + 1])
                else:
                    last = nc.scalar.activation(y[0:1, :, first:end],
                                                acc[n % 2][0:1, 0:w].rearrange("a (t p) -> a p t", p=P), ACT.Copy)
                last.then_inc(acc_kept, 1)

            act.wait_ge(rest_landed, 64)
            def pairs_moved(t, k):
                g = GANGS * t + k
                act.wait_ge(gram_ready, g + 1)
                if k % 2 == 0 and 0 < t < T - 1:
                    act.wait_ge(pairs_split, 2 * (t - 1) + k // 2 + 1)
                if k == 0 and t == T - 1:
                    act.wait_ge(acc_ready, acc_number["one", 1, O1 - 1] + 1)
                for s in (0, 1):
                    for q in range(NQ):
                        w = min(CH, M - CH * q)
                        last = nc.scalar.activation(pair_place(s, q, w, g), gram_block(s, q, w, g), ACT.Copy)
                last.then_inc(moved_act, 1)

            def weights_high(o):
                if o == 0:
                    act.wait_ge(turned_ready, number["hot", S - 2, None] + 1)
                    act.wait_ge(w1_landed, 16 * (M + 2))
                    act.wait_ge(w1_ready, 1)
                oc = slice(o * P, o * P + P)
                nc.scalar.activation(w1_hi[:, :, oc], w1[:, :, oc], ACT.Copy).then_inc(w1_hi_ready, 1)

            for kind, a, i in steps:
                if kind == "turn":
                    if by_act[number["group", a, i]]:
                        keep(number["group", a, i])
                elif kind == "gram":
                    pairs_moved(a, i)
                elif kind == "parts":
                    weights_high(a)
                elif kind in ("one", "two", "three"):
                    if (kind, a) == ("one", 0) and i < T - 2:
                        pads(i + 2)
                    layer_kept(kind, a, i)

        @block.tensor
        def _(pe):
            def bank_free(n):
                before = [m for m in range(n) if bank_key(m) == bank_key(n)]
                if before:
                    pe.wait_ge(*kept[before[-1]])

            def spread_ids(s):
                if s >= 2:
                    pe.wait_ge(acc_kept, s - 1)
                for t in range(T):
                    col = ids_h[:, t, ONE_HOT[s]:ONE_HOT[s] + 1]
                    last = nc.tensor.matmul(acc[s % 2][:, t * P:t * P + P], col.to_broadcast([P, P]), ident_h[:],
                                            start=True, stop=True)
                last.then_inc(acc_ready, 1)

            pe.wait_ge(pairs_zero, 1)
            for i in range(WARM):
                nc.tensor.matmul(gram[1][:, 0, :], pairs[:, 0, :], pairs[:, 1, :], start=True, stop=True)
            pe.wait_ge(consts_ready, 1)
            spread_ids(0)
            pe.wait_ge(ident_ready, 1)
            pe.wait_ge(dense_landed, 16)
            for t in range(T):
                last = nc.tensor.transpose(bank(0)[:, t, :], dense_r[:, t, :], ident[:])
            last.then_inc(turned_ready, 1)

            at = {f: i for i, f in enumerate(gathered)}

            def turn(t, j):
                n = number["group", t, j]
                bank_free(n)
                pe.wait_ge(group_landed[t][j], 16 * len(groups[j]))
                for i, f in enumerate(groups[j]):
                    last = nc.tensor.transpose(bank(n)[:, i, :], rows[:, t % 2, at[f], :], ident[:])
                last.then_inc(turned_ready, 1)

            def layer(kind, batch, o):
                n = acc_number[kind, batch, o]
                first, end = BATCHES[batch]
                w = (end - first) * P
                oc = slice(o * P, o * P + P)
                pe.wait_ge(acc_kept, n - 1)
                if kind == "one":
                    for c in (CH, *range(CH)):
                        if batch == 0 and c == CH:
                            pe.wait_ge(w1_lo_ready, o + 1)
                            pe.wait_ge(dense_split, 2)
                        if o == 0 and batch == 0 and c == 0:
                            pe.wait_ge(pairs_split, 2 * end)
                        if o == 0 and batch and c == 0:
                            pe.wait_ge(moved_act, GANGS * end)
                            pe.wait_ge(moved_dve, GANGS * end)
                        if o == 0 and batch == 1 and c == CH:
                            pe.wait_ge(w1_ready, 1)
                        begin, done = c == CH, c == CH - 1
                        if batch:
                            x = pairs[:, c, :] if c < CH else dense_t[:, first * P:end * P]
                            last = nc.tensor.matmul(acc[n % 2][:, 0:w], w1[:, c, oc], x, start=begin, stop=done)
                            continue
                        if c < CH:
                            x_hi, x_lo = pairs_hi[:, c, :], pairs_lo[:, c, :]
                        else:
                            x_hi, x_lo = dense_hi[:], dense_lo[:]
                        nc.tensor.matmul(acc[n % 2][:, 0:w], w1_hi[:, c, oc], x_hi, start=begin, stop=False)
                        nc.tensor.matmul(acc[n % 2][:, 0:w], w1_hi[:, c, oc], x_lo, start=False, stop=False)
                        last = nc.tensor.matmul(acc[n % 2][:, 0:w], w1_lo[:, c, oc], x_hi, start=False, stop=done)
                elif kind == "two":
                    for c in range(O1):
                        if o == 0:
                            pe.wait_ge(acc_kept, acc_number["one", batch, c] + 1)
                        last = nc.tensor.matmul(acc[n % 2][:, 0:w], w2[:, c, oc], h1[:, c, 0:w],
                                                start=(c == 0), stop=(c == O1 - 1))
                else:
                    for c in range(O2):
                        pe.wait_ge(acc_kept, acc_number["two", batch, c] + 1)
                        last = nc.tensor.matmul(acc[n % 2][0:1, 0:w], w3[:, c:c + 1], h2[:, c, 0:w],
                                                start=(c == 0), stop=(c == O2 - 1))
                last.then_inc(acc_ready, 1)

            for s in range(S):
                if s + 1 < S:
                    spread_ids(s + 1)
                for j in EARLY.get(s, ()):
                    turn(0, j)
                n = number["hot", s, None]
                bank_free(n)
                for part in (table_hi, table_lo):
                    for c in range(TC[s]):
                        if part is table_hi and c < TC[s] - BY_ACT[s]:
                            pe.wait_ge(hot_ready, hot_by_dve(s) + c + 1)
                        elif part is table_hi:
                            pe.wait_ge(hot_ready_act, sum(BY_ACT[:s]) + c - (TC[s] - BY_ACT[s]) + 1)
                        if c == 0:
                            pe.wait_ge(hi_ready if part is table_hi else lo_ready, s + 1)
                        last = nc.tensor.matmul(bank(n), part[0:TP[s], s % 2, c, :],
                                                one_hot[0:TP[s], s % 2, c, :],
                                                start=(c == 0 and part is table_hi),
                                                stop=(c == TC[s] - 1 and part is table_lo))
                last.then_inc(turned_ready, 1)

            def gram_products(t, k):
                g = GANGS * t + k
                if k == 0:
                    n = number["group", t, NG - 1]
                    pe.wait_ge(*kept[n])
                    pe.wait_ge(*kept[n - 1])
                    if t == 0:
                        pe.wait_ge(*kept[number["hot", S - 1, None]])
                    pe.wait_ge(pads_ready, t + 1)
                if g >= 2:
                    pe.wait_ge(moved_act, g - 1)
                    pe.wait_ge(moved_dve, g - 1)
                for i in range(SPAN):
                    first = (k * SPAN + i) * 4
                    four = vecs_t[:, t, first:first + 4, :]
                    last = nc.tensor.matmul(gram[g % 2][:, i, 0:4 * M].rearrange("n (s m) -> n s m", m=M),
                                            four.rearrange("d s n -> d (s n)"), four[:, :, 0:M],
                                            start=True, stop=True)
                last.then_inc(gram_ready, 1)

            pe.wait_ge(rest_landed, 64)
            for kind, a, i in steps:
                if kind == "turn":
                    turn(a, i)
                elif kind == "gram":
                    gram_products(a, i)
                elif kind in ("one", "two", "three"):
                    layer(kind, a, i)


def kernel(**inputs):
    import numpy as _np
    import concourse.bacc as _bacc
    from concourse import mybir as _mybir
    from concourse.bass_utils import run_bass_kernel_spmd as _run

    nc = _bacc.Bacc("TRN2", target_bir_lowering=False, num_devices=1)
    arrays, aps = {}, {}
    for name, value in inputs.items():
        a = _np.ascontiguousarray(value)
        arrays[f"in_{name}"] = a
        aps[name] = nc.dram_tensor(f"in_{name}", a.shape, _mybir.dt.from_np(a.dtype), kind="ExternalInput").ap()
    batch, fields = arrays["in_ids"].shape
    out = nc.dram_tensor("out_y", (batch, 1), _mybir.dt.float32, kind="ExternalOutput").ap()
    dlrm_tower(nc, aps["r_dense_features"], aps["ids"], [aps[f"tbl_{f}"] for f in range(fields)],
               aps["W_top1"], aps["b_top1"], aps["W_top2"], aps["b_top2"], aps["W_top3"], out)
    r = _run(nc, [arrays], core_ids=[0])
    return r.results[0]["out_y"]
```

```python
from contextlib import ExitStack

import concourse.bass as bass
from concourse import mybir

F32 = mybir.dt.float32
F32R = mybir.dt.float32r
F16 = mybir.dt.float16
I32 = mybir.dt.int32
U32 = mybir.dt.uint32
ALU = mybir.AluOpType
ACT = mybir.ActivationFunctionType

P = 128
QUAD = 32
ONE_HOT = (0, 2, 4, 6, 7, 8, 9)


def runs(fields):
    out, i = [], 0
    while i < len(fields):
        step = fields[i + 1] - fields[i] if i + 1 < len(fields) else 1
        n = 1
        while i + n < len(fields) and fields[i + n] - fields[i + n - 1] == step:
            n += 1
        out.append((i, fields[i], step, n))
        i += n
    return out


def dlrm_tower(nc, dense, ids, tables, w_top1, b_top1, w_top2, b_top2, w_top3, out):
    B, D = dense.shape
    F = ids.shape[1]
    N = F + 1
    T = B // P
    H1, H2 = w_top1.shape[1], w_top2.shape[1]
    O1, O2 = H1 // P, H2 // P
    NQ = P // QUAD
    CH = 5
    CUT = NQ * CH
    LOWER = ((0, 0, CUT, CH, N), (1, 0, CUT + CH, 1, N), (2, 0, 2 * CH, CH, N), (3, 0, 3 * CH, CH, N))
    UPPER = ((0, 0, 0, CH, CUT), (1, 0, CH, CH, N - 1), (2, 0, CUT, CH, CH), (3, 0, CUT + CH, 2, 2 * CH))
    held = {}
    for q, c, col, w, height in LOWER + UPPER:
        held.update({(CH * q + c + i, n): col + i for i in range(w) for n in range(height)})
    place = {}
    for (slot, n), col in sorted(held.items()):
        if n != col:
            place.setdefault((min(n, col), max(n, col)), []).append((n < col, slot, n))
    place = {pair: min(where)[1:] for pair, where in place.items()}
    assert len(place) == N * (N - 1) // 2
    W1_RUNS = []
    for at, pair in enumerate((i, j) for i in range(N) for j in range(i + 1, N)):
        slot, n = place[pair]
        if W1_RUNS:
            first, slot0, n0, down, count = W1_RUNS[-1]
            if slot == slot0 and n == n0 + count and (down or count == 1):
                W1_RUNS[-1] = (first, slot0, n0, True, count + 1)
                continue
            if slot // CH == slot0 // CH and slot == slot0 + count and n == n0 and (count == 1 or not down):
                W1_RUNS[-1] = (first, slot0, n0, False, count + 1)
                continue
        W1_RUNS.append((at, slot, n, True, 1))
    PER_TABLE = 6
    assert D == P and B == T * P and N <= QUAD

    gathered = [f for f in range(F) if f not in ONE_HOT]
    groups = [gathered[i:i + 4] for i in range(0, len(gathered), 4)]
    NG = len(groups)
    S = len(ONE_HOT)
    TP = [max(p for p in range(1, P + 1) if tables[f].shape[0] % p == 0) for f in ONE_HOT]
    TC = [tables[f].shape[0] // p for f, p in zip(ONE_HOT, TP)]
    assert max(tables[f].shape[0] for f in ONE_HOT) <= 2048
    TPX, TCX = max(TP), max(TC)

    C1 = CH + 1
    assert T == 4

    WARM = 5
    SPAN = 8
    GANGS = P // (4 * SPAN)

    with ExitStack() as ctx:
        def sb(name, shape, dt):
            return ctx.enter_context(nc.sbuf_tensor(name, shape, dt))

        def ps(name, shape, dt):
            return ctx.enter_context(nc.psum_tensor(name, shape, dt))

        def sem(name):
            return ctx.enter_context(nc.semaphore(name))

        ids_i = sb("ids_i", [P, T, F], I32)
        ids_h = sb("ids_h", [P, T, F], F16)
        ident = sb("ident", [P, P], F32)
        ident_h = sb("ident_h", [P, P], F16)
        row_of = {tc: sb(f"row_of{tc}", [P, tc], F32) for tc in sorted(set(TC))}
        row_of_i = {tc: sb(f"row_of_i{tc}", [P, tc], I32) for tc in sorted(set(TC))}
        dense_r = sb("dense_r", [P, T, D], F32)
        dense_t = sb("dense_t", [P, B], F32)
        rows = sb("rows", [P, 2, len(gathered), D], F32)
        table = sb("table", [TPX, 2, TCX, D], F32)
        table_hi = sb("table_hi", [TPX, 2, TCX, D], F32R)
        table_lo = sb("table_lo", [TPX, 2, TCX, D], F32R)
        ids_bc = sb("ids_bc", [P, 2, B], F32)
        one_hot = sb("one_hot", [P, 2, TCX, B], F32R)
        vecs_t = sb("vecs_t", [P, T, P, QUAD], F32)
        pairs = sb("pairs", [P, 2, CH, P], F32)
        w1 = sb("w1", [P, C1, H1], F32)
        w1_last = sb("w1_last", [P, H1], F32)
        w2 = sb("w2", [P, O1, H2], F32)
        w3 = sb("w3", [P, O2], F32)
        b1 = sb("b1", [P, O1], F32)
        b2 = sb("b2", [P, O2], F32)
        h1 = sb("h1", [P, O1, P], F32)
        assert O1 * P == B and O2 == 2
        square = h1[:].rearrange("p o b -> p (o b)")
        h2 = ids_bc[:, :, 0:P]
        y = sb("y", [1, P, T], F32)

        turned = [ps(f"turned{i}", [P, 4, P], F32) for i in range(2)]
        gram = [ps(f"gram{i}", [P, SPAN, P], F32) for i in range(2)]
        acc = [ps(f"acc{i}", [P, B], F32) for i in range(2)]

        ids_landed = sem("ids_landed")
        dense_landed = sem("dense_landed")
        table_landed = [sem(f"table_landed{s}") for s in range(S)]
        group_landed = [[sem(f"group_landed{t}_{j}") for j in range(NG)] for t in range(T)]
        w1_landed = sem("w1_landed")
        rest_landed = sem("rest_landed")
        ident_zero = sem("ident_zero")
        ident_ready = sem("ident_ready")
        iota_ready = sem("iota_ready")
        consts_ready = sem("consts_ready")
        pairs_zero = sem("pairs_zero")
        pads_ready = sem("pads_ready")
        w1_zero = sem("w1_zero")
        w1_ready = sem("w1_ready")
        acc_ready = sem("acc_ready")
        acc_kept = sem("acc_kept")
        hi_ready = sem("hi_ready")
        lo_ready = sem("lo_ready")
        hot_ready = sem("hot_ready")
        hot_square = sem("hot_square")
        hot_ready_act = sem("hot_ready_act")
        turned_ready = sem("turned_ready")
        kept_act = sem("kept_act")
        kept_dve = sem("kept_dve")
        gram_ready = sem("gram_ready")
        lower_act = sem("lower_act")
        lower_dve = sem("lower_dve")
        moved_act = sem("moved_act")
        moved_dve = sem("moved_dve")
        out_written = sem("out_written")

        EARLY = {S - NG + 1 + j: (j,) for j in range(NG - 2)} | {S - 1: (NG - 2, NG - 1)}
        uses = [("dense", None, None)]
        for s in range(S):
            uses += [("group", 0, j) for j in EARLY.get(s, ())] + [("hot", s, None)]
        uses += [("group", t, j) for t in range(1, T) for j in range(NG)]
        number = {u: n for n, u in enumerate(uses)}
        by_act = [u[0] != "group" or u[1:] < (T - 1, 0) or n % 2 == 0 for n, u in enumerate(uses)]
        kept = {}
        for n, u in enumerate(uses):
            same = by_act[:n + 1].count(by_act[n])
            kept[n] = (kept_act if by_act[n] else kept_dve, same)

        work = []
        for t in range(T):
            gangs = [("gram", t, k) for k in range(GANGS)]
            one = [("one", t, o) for o in range(O1)]
            if t == 0:
                work.append([*gangs, ("gram", 1, 0), *one])
            else:
                two = [("two", t - 1, o) for o in range(O2)]
                work.append([*gangs[t == 1:], *two, one[0], ("three", t - 1, 0), *one[1:]])
        work.append([("two", T - 1, o) for o in range(O2)] + [("three", T - 1, 0)])
        TURN_AT = ((0, 0, 1, 2, 3), (1, 2, 3, 4, 8), (1, 2, 4, 8, 10))
        steps = []
        for t, pieces in enumerate(work):
            for i in range(len(pieces) + 1):
                steps += [("turn", t + 1, j) for j in range(NG) if TURN_AT[t][j] == i] if t < T - 1 else []
                steps += pieces[i:i + 1]
        acc_uses = [("ids", s, None) for s in range(S)] + [u for u in steps if u[0] in ("one", "two", "three")]
        acc_number = {u: n for n, u in enumerate(acc_uses)}
        assert [u for u in steps if u[0] == "turn"] == [("turn", t, j) for t in range(1, T) for j in range(NG)]

        def bank_key(n):
            kind, t, j = uses[n]
            if (kind, t) == ("group", 0):
                return 1, j % 4
            return 0, sum(u[:2] != ("group", 0) for u in uses[:n]) % 2

        def bank(n):
            which, i = bank_key(n)
            return gram[i // 2][:, i % 2 * 4:i % 2 * 4 + 4, :] if which else turned[i][:]

        def vec_slots(t, n, step, count):
            v = vecs_t[:, t].rearrange("d b n -> d n b")
            return v[:, n:n + step * (count - 1) + 1:step, :]

        def gram_block(s, part, g):
            _, _, col, w, height = part
            return gram[g % 2][QUAD * s:QUAD * s + height, :, s * N + col:s * N + col + w].rearrange("n k c -> n c k")

        def pair_place(s, part, g):
            q, c, _, w, height = part
            t, k = divmod(g, GANGS)
            b = k * SPAN * 4
            return pairs[QUAD * q:QUAD * q + height, t % 2, c:c + w, b + s:b + 4 * SPAN:4]

        def hot_by_dve(s):
            return sum(TC[:s]) - s

        block = ctx.enter_context(nc.Block())

        @block.sync
        def _(sp):
            sp.dma_start(ids_i[:], ids.rearrange("(p t) f -> p t f", t=T)).then_inc(ids_landed, 16)

            def load_table(s):
                src = tables[ONE_HOT[s]].rearrange("(p c) d -> p c d", c=TC[s])
                cut = TP[s] // 16 * 16
                if s >= 2:
                    sp.wait_ge(hi_ready, s - 1)
                    sp.wait_ge(lo_ready, s - 1)
                sp.dma_start(table[0:cut, s % 2, 0:TC[s], :], src[0:cut]).then_inc(table_landed[s], 16)
                sp.dma_start(table[cut:TP[s], s % 2, 0:TC[s], :], src[cut:TP[s]]).then_inc(table_landed[s], 16)

            def load_w1(run):
                at, slot, n, down, count = run
                q, c = divmod(slot, CH)
                to = w1[QUAD * q + n:QUAD * q + n + (count if down else 1), c:c + (1 if down else count), :]
                src = w_top1[D + at:D + at + count, :].rearrange("(n c) h -> n c h", c=1 if down else count)
                sp.dma_start(to, src).then_inc(w1_landed, 16)

            load_table(0)
            sp.dma_start(dense_r[:], dense.rearrange("(p t) d -> p t d", t=T)).then_inc(dense_landed, 16)
            load_table(1)
            sp.wait_ge(pairs_zero, 1)
            sp.dma_start(w1[:, 0:CH, :], pairs[:, 0, 0:H1 // P, :].rearrange("p (a c) b -> p a (c b)", a=1)
                         .to_broadcast([P, CH, H1])).then_inc(w1_zero, 16)
            sp.wait_ge(w1_zero, 16)
            for s in range(2, S):
                load_table(s)
                for run in W1_RUNS[PER_TABLE * (s - 2):PER_TABLE * (s - 1)]:
                    load_w1(run)
            for run in W1_RUNS[PER_TABLE * (S - 2):]:
                load_w1(run)
            sp.dma_start(w1[:, CH, :], w_top1[0:D, :]).then_inc(w1_landed, 16)
            sp.dma_start(w1_last[:], w_top1[w_top1.shape[0] - D:, :]).then_inc(w1_landed, 16)
            sp.dma_start(w2[:], w_top2.rearrange("(c p) n -> p c n", p=P)).then_inc(rest_landed, 16)
            with nc.allow_non_contiguous_dma(reason="biases and a column, one element per partition"):
                sp.dma_start(b1[:], b_top1.rearrange("(c p) -> p c", p=P)).then_inc(rest_landed, 16)
                sp.dma_start(b2[:], b_top2.rearrange("(c p) -> p c", p=P)).then_inc(rest_landed, 16)
                sp.dma_start(w3[:], w_top3.rearrange("(c p) o -> p (c o)", p=P)).then_inc(rest_landed, 16)
            sp.wait_ge(acc_kept, len(acc_uses))
            sp.dma_start(out.rearrange("(a b) o -> a (b o)", a=1),
                         y[:].rearrange("a p t -> a (p t)")).then_inc(out_written, 16)
            sp.wait_ge(out_written, 16)

        @block.gpsimd
        def _(pool):
            pool.memset(ident[:], 0.0).then_inc(ident_zero, 1)
            pool.wait_ge(ident_zero, 1)
            pool.affine_select(out=ident[:], in_=ident[:], compare_op=ALU.not_equal, fill=1.0, base=0,
                               pattern=[[-1, P]], channel_multiplier=1).then_inc(ident_ready, 1)
            for tc in sorted(row_of):
                pool.iota(row_of_i[tc][:], pattern=[[1, tc]], base=0, channel_multiplier=tc).then_inc(iota_ready, 1)
            pool.wait_ge(ids_landed, 16)
            for t in range(T):
                for j, group in enumerate(groups):
                    if t >= 2:
                        pool.wait_ge(turned_ready, number["group", t - 2, j] + 1)
                    for f in group:
                        pool.indirect_dma_start(
                            rows[:, t % 2, gathered.index(f), :], None, tables[f],
                            bass.IndirectOffsetOnAxis(ap=ids_i[:, t, f:f + 1].bitcast(U32), axis=0),
                        ).then_inc(group_landed[t][j], 16)

        @block.vector
        def _(dve):
            nc.vector.memset(pairs[:, 0], 0.0).then_inc(pairs_zero, 1)
            nc.vector.memset(pairs[:, 1], 0.0)
            dve.wait_ge(iota_ready, len(row_of))
            for tc in sorted(row_of):
                nc.vector.tensor_copy(row_of[tc][:], row_of_i[tc][:])
            dve.wait_ge(ident_ready, 1)
            nc.vector.tensor_copy(ident_h[:], ident[:])
            dve.wait_ge(ids_landed, 16)
            nc.vector.tensor_scalar(ids_h[:], ids_i[:], 2047.0, None, ALU.min).then_inc(consts_ready, 1)
            dve.wait_ge(consts_ready, 1)
            for s in range(S):
                dve.wait_ge(acc_kept, s + 1)
                if s >= 2:
                    dve.wait_ge(turned_ready, number["hot", s - 2, None] + 1)
                for c in range(TC[s] - 1):
                    nc.vector.tensor_scalar(one_hot[0:TP[s], s % 2, c, :], ids_bc[0:TP[s], s % 2, :],
                                            row_of[TC[s]][0:TP[s], c:c + 1], None,
                                            ALU.is_equal).then_inc(hot_ready, 1)
                    if c == 3:
                        dve.wait_ge(hi_ready, s + 1)
                        nc.vector.tensor_tensor(table_lo[0:TP[s], s % 2, 0:TC[s], :],
                                                table[0:TP[s], s % 2, 0:TC[s], :],
                                                table_hi[0:TP[s], s % 2, 0:TC[s], :],
                                                ALU.subtract).then_inc(lo_ready, 1)
            dve.wait_ge(w1_landed, 16 * (len(W1_RUNS) + 2))
            nc.vector.tensor_tensor(w1[:, CH, :], w1[:, CH, :], w1_last[:], ALU.add).then_inc(w1_ready, 1)

            def turned_kept(t, j):
                n = number["group", t, j]
                if not by_act[n]:
                    dve.wait_ge(turned_ready, n + 1)
                    for at, f, step, count in runs(groups[j]):
                        last = nc.vector.tensor_copy(vec_slots(t, f + 1, step, count),
                                                     bank(n)[:, at:at + count, :])
                    last.then_inc(kept_dve, 1)

            def pairs_moved(t, k):
                g = GANGS * t + k
                dve.wait_ge(gram_ready, g + 1)
                if k == 0 and t >= 2:
                    dve.wait_ge(acc_ready, acc_number["one", t - 2, O1 - 1] + 1)
                for s in (2, 3):
                    for part in LOWER:
                        last = nc.vector.tensor_copy(pair_place(s, part, g), gram_block(s, part, g))
                    last.then_inc(lower_dve, 1)
                for i, s in enumerate((2, 3)):
                    dve.wait_ge(lower_dve, 2 * g + i + 1)
                    for part in UPPER:
                        last = nc.vector.tensor_copy(pair_place(s, part, g), gram_block(s, part, g))
                last.then_inc(moved_dve, 1)

            for kind, a, i in steps:
                if kind == "turn":
                    turned_kept(a, i)
                elif kind == "gram":
                    pairs_moved(a, i)

        @block.scalar
        def _(act):
            def keep(n):
                kind, a, j = uses[n]
                act.wait_ge(turned_ready, n + 1)
                if kind == "dense":
                    for t in range(T):
                        nc.scalar.activation(vec_slots(t, 0, 1, 1), bank(n)[:, t:t + 1, :], ACT.Copy)
                    last = nc.scalar.activation(dense_t[:].rearrange("d (t b) -> d t b", t=T), bank(n), ACT.Copy)
                elif kind == "hot":
                    v = vecs_t[:, :, :, ONE_HOT[a] + 1]
                    last = nc.scalar.activation(v, bank(n), ACT.Copy)
                else:
                    for at, f, step, count in runs(groups[j]):
                        last = nc.scalar.activation(vec_slots(a, f + 1, step, count),
                                                    bank(n)[:, at:at + count, :], ACT.Copy)
                last.then_inc(kept_act, 1)

            def spread_kept(s):
                act.wait_ge(acc_ready, s + 1)
                if s >= 2:
                    act.wait_ge(hot_ready, hot_by_dve(s - 1))
                nc.scalar.activation(ids_bc[:, s % 2, :], acc[s % 2][:], ACT.Copy).then_inc(acc_kept, 1)

            def hots_last(s):
                act.wait_ge(acc_kept, s + 1)
                if s == 0:
                    act.wait_ge(consts_ready, 1)
                if s >= 2:
                    act.wait_ge(turned_ready, number["hot", s - 2, None] + 1)
                if s:
                    act.wait_ge(hot_ready_act, s)
                c = TC[s] - 1
                nc.scalar.activation(square[0:TP[s], :], ids_bc[0:TP[s], s % 2, :], ACT.Square, scale=-1.0,
                                     bias=row_of[TC[s]][0:TP[s], c:c + 1]).then_inc(hot_square, 1)
                act.wait_ge(hot_square, s + 1)
                nc.scalar.activation(one_hot[0:TP[s], s % 2, c, :], square[0:TP[s], :], ACT.Relu,
                                     scale=-1.0, bias=1.0).then_inc(hot_ready_act, 1)

            def table_high(s):
                act.wait_ge(table_landed[s], 32)
                if s >= 2:
                    act.wait_ge(turned_ready, number["hot", s - 2, None] + 1)
                nc.scalar.activation(table_hi[0:TP[s], s % 2, 0:TC[s], :], table[0:TP[s], s % 2, 0:TC[s], :],
                                     ACT.Copy).then_inc(hi_ready, 1)

            spread_kept(0)
            table_high(0)
            hots_last(0)
            keep(0)
            spread_kept(1)
            table_high(1)
            hots_last(1)
            act.wait_ge(ident_ready, 1)

            def pads(t):
                zero = ident[:].rearrange("p (a b) -> p a b", a=1).to_broadcast([P, QUAD - N, P])
                nc.scalar.activation(vecs_t[:, t, :, N:QUAD].rearrange("d b n -> d n b"), zero,
                                     ACT.Copy, scale=0.0).then_inc(pads_ready, 1)

            for s in range(1, S):
                if s + 1 < S:
                    spread_kept(s + 1)
                keep(number["hot", s - 1, None])
                for j in EARLY.get(s, ()):
                    keep(number["group", 0, j])
                if s + 1 < S:
                    table_high(s + 1)
                    hots_last(s + 1)
                if s <= T:
                    pads(s - 1)
            keep(number["hot", S - 1, None])

            def layer_kept(kind, t, o):
                n = acc_number[kind, t, o]
                act.wait_ge(acc_ready, n + 1)
                if (kind, t, o) == ("one", 0, 0):
                    act.wait_ge(rest_landed, 64)
                if kind == "one":
                    last = nc.scalar.activation(h1[:, o, :], acc[n % 2][:, 0:P], ACT.Relu, bias=b1[:, o:o + 1])
                elif kind == "two":
                    last = nc.scalar.activation(h2[:, o, :], acc[n % 2][:, 0:P], ACT.Relu, bias=b2[:, o:o + 1])
                else:
                    last = nc.scalar.activation(y[0:1, :, t], acc[n % 2][0:1, 0:P], ACT.Copy)
                last.then_inc(acc_kept, 1)

            def pairs_moved(t, k):
                g = GANGS * t + k
                act.wait_ge(gram_ready, g + 1)
                if k == 0 and t >= 2:
                    act.wait_ge(acc_ready, acc_number["one", t - 2, O1 - 1] + 1)
                for s in (0, 1):
                    for part in LOWER:
                        last = nc.scalar.activation(pair_place(s, part, g), gram_block(s, part, g), ACT.Copy)
                    last.then_inc(lower_act, 1)
                for i, s in enumerate((0, 1)):
                    act.wait_ge(lower_act, 2 * g + i + 1)
                    for part in UPPER:
                        last = nc.scalar.activation(pair_place(s, part, g), gram_block(s, part, g), ACT.Copy)
                last.then_inc(moved_act, 1)

            for kind, a, i in steps:
                if kind == "turn":
                    if by_act[number["group", a, i]]:
                        keep(number["group", a, i])
                elif kind == "gram":
                    pairs_moved(a, i)
                elif kind in ("one", "two", "three"):
                    layer_kept(kind, a, i)

        @block.tensor
        def _(pe):
            def bank_free(n):
                before = [m for m in range(n) if bank_key(m) == bank_key(n)]
                if before:
                    pe.wait_ge(*kept[before[-1]])

            def spread_ids(s):
                if s >= 2:
                    pe.wait_ge(acc_kept, s - 1)
                for t in range(T):
                    col = ids_h[:, t, ONE_HOT[s]:ONE_HOT[s] + 1]
                    last = nc.tensor.matmul(acc[s % 2][:, t * P:t * P + P], col.to_broadcast([P, P]), ident_h[:],
                                            start=True, stop=True)
                last.then_inc(acc_ready, 1)

            pe.wait_ge(pairs_zero, 1)
            for i in range(WARM):
                nc.tensor.matmul(gram[1][:, 0, :], pairs[:, 0, 0, :], pairs[:, 0, 1, :], start=True, stop=True)
            pe.wait_ge(consts_ready, 1)
            spread_ids(0)
            pe.wait_ge(ident_ready, 1)
            pe.wait_ge(dense_landed, 16)
            for t in range(T):
                last = nc.tensor.transpose(bank(0)[:, t, :], dense_r[:, t, :], ident[:])
            last.then_inc(turned_ready, 1)

            def turn(t, j):
                n = number["group", t, j]
                bank_free(n)
                pe.wait_ge(group_landed[t][j], 16 * len(groups[j]))
                for i, f in enumerate(groups[j]):
                    last = nc.tensor.transpose(bank(n)[:, i, :], rows[:, t % 2, gathered.index(f), :], ident[:])
                last.then_inc(turned_ready, 1)

            def layer(kind, t, o):
                n = acc_number[kind, t, o]
                oc = slice(o * P, o * P + P)
                pe.wait_ge(acc_kept, n - 1)
                if kind == "one":
                    if (t, o) == (0, 0):
                        pe.wait_ge(w1_ready, 1)
                    nc.tensor.matmul(acc[n % 2][:, 0:P], w1[:, CH, oc], dense_t[:, t * P:t * P + P],
                                     start=True, stop=False)
                    if o == 0:
                        pe.wait_ge(moved_act, GANGS * (t + 1))
                        pe.wait_ge(moved_dve, GANGS * (t + 1))
                    for c in range(CH):
                        last = nc.tensor.matmul(acc[n % 2][:, 0:P], w1[:, c, oc], pairs[:, t % 2, c, :],
                                                start=False, stop=(c == CH - 1))
                elif kind == "two":
                    if (t, o) == (0, 0):
                        pe.wait_ge(rest_landed, 64)
                    for c in range(O1):
                        if o == 0:
                            pe.wait_ge(acc_kept, acc_number["one", t, c] + 1)
                        last = nc.tensor.matmul(acc[n % 2][:, 0:P], w2[:, c, oc], h1[:, c, :],
                                                start=(c == 0), stop=(c == O1 - 1))
                else:
                    for c in range(O2):
                        pe.wait_ge(acc_kept, acc_number["two", t, c] + 1)
                        last = nc.tensor.matmul(acc[n % 2][0:1, 0:P], w3[:, c:c + 1], h2[:, c, :],
                                                start=(c == 0), stop=(c == O2 - 1))
                last.then_inc(acc_ready, 1)

            for s in range(S):
                if s + 1 < S:
                    spread_ids(s + 1)
                for j in EARLY.get(s, ()):
                    turn(0, j)
                n = number["hot", s, None]
                bank_free(n)
                for part in (table_hi, table_lo):
                    for c in range(TC[s]):
                        if part is table_hi and c < TC[s] - 1:
                            pe.wait_ge(hot_ready, hot_by_dve(s) + c + 1)
                        elif part is table_hi:
                            pe.wait_ge(hot_ready_act, s + 1)
                        if c == 0:
                            pe.wait_ge(hi_ready if part is table_hi else lo_ready, s + 1)
                        last = nc.tensor.matmul(bank(n)[:], part[0:TP[s], s % 2, c, :],
                                                one_hot[0:TP[s], s % 2, c, :],
                                                start=(c == 0 and part is table_hi),
                                                stop=(c == TC[s] - 1 and part is table_lo))
                last.then_inc(turned_ready, 1)

            def gram_products(t, k):
                g = GANGS * t + k
                if k == 0:
                    n = number["group", t, NG - 1]
                    pe.wait_ge(*kept[n])
                    pe.wait_ge(*kept[n - 1])
                    if t == 0:
                        pe.wait_ge(*kept[number["hot", S - 1, None]])
                    pe.wait_ge(pads_ready, t + 1)
                if g >= 2:
                    pe.wait_ge(moved_act, g - 1)
                    pe.wait_ge(moved_dve, g - 1)
                for i in range(SPAN):
                    first = (k * SPAN + i) * 4
                    four = vecs_t[:, t, first:first + 4, :]
                    last = nc.tensor.matmul(gram[g % 2][:, i, 0:4 * N].rearrange("n (s m) -> n s m", m=N),
                                            four.rearrange("d s n -> d (s n)"), four[:, :, 0:N],
                                            start=True, stop=True)
                last.then_inc(gram_ready, 1)

            for kind, a, i in steps:
                if kind == "turn":
                    turn(a, i)
                elif kind == "gram":
                    gram_products(a, i)
                elif kind in ("one", "two", "three"):
                    layer(kind, a, i)


def kernel(**inputs):
    import numpy as _np
    import concourse.bacc as _bacc
    from concourse import mybir as _mybir
    from concourse.bass_utils import run_bass_kernel_spmd as _run

    nc = _bacc.Bacc("TRN2", target_bir_lowering=False, num_devices=1)
    arrays, aps = {}, {}
    for name, value in inputs.items():
        a = _np.ascontiguousarray(value)
        arrays[f"in_{name}"] = a
        aps[name] = nc.dram_tensor(f"in_{name}", a.shape, _mybir.dt.from_np(a.dtype), kind="ExternalInput").ap()
    batch, fields = arrays["in_ids"].shape
    out = nc.dram_tensor("out_y", (batch, 1), _mybir.dt.float32, kind="ExternalOutput").ap()
    dlrm_tower(nc, aps["r_dense_features"], aps["ids"], [aps[f"tbl_{f}"] for f in range(fields)],
               aps["W_top1"], aps["b_top1"], aps["W_top2"], aps["b_top2"], aps["W_top3"], out)
    r = _run(nc, [arrays], core_ids=[0])
    return r.results[0]["out_y"]
```
